# Optimizing a Trainium2 kernel written in Bass

```python
import numpy as np
import jax
import jax.numpy as jnp

def _softmax(x, axis=-1):
    return jax.nn.softmax(x, axis=axis)

def _gelu(x):
    return jax.nn.gelu(x, approximate=True)

def _silu(x):
    return jax.nn.silu(x)

def _sigmoid(x):
    return jax.nn.sigmoid(x)

def _layernorm(x, axis=-1, eps=1e-05):
    m = jnp.mean(x, axis=axis, keepdims=True)
    v = jnp.var(x, axis=axis, keepdims=True)
    return (x - m) / jnp.sqrt(v + eps)

def _scatter_add(tgt, idx, src, axis=0):
    return tgt.at[idx].add(src)

def _segment_sum(src, seg, n):
    return jax.ops.segment_sum(src, seg, n)
kernel_name = 'mk_dlrm_tower_d1_rec_r8_1f0086'

def setup_inputs(seed: int=0):
    np.random.seed(seed)
    _w = jnp.asarray

    def _rec_inputs():
        import jax
        import jax.numpy as jnp
        _tk = jax.random.key(seed)
        ids = jnp.stack([jax.random.randint(jax.random.fold_in(_tk, 200 + f), (2048,), 0, v, jnp.int32) for f, v in enumerate([1000, 1250, 1250, 1250, 1250, 1250, 12500, 1250, 12500, 12500, 125000, 12500, 1250, 1250, 1250, 12500, 1250, 12500, 12500, 1250, 1000, 1000, 12500, 1250, 1250, 1000])], axis=1)
        tbl_0 = 0.05 * jax.random.normal(jax.random.fold_in(_tk, 500 + 0), (1000, 128), jnp.float32)
        tbl_1 = 0.05 * jax.random.normal(jax.random.fold_in(_tk, 500 + 1), (1250, 128), jnp.float32)
        tbl_2 = 0.05 * jax.random.normal(jax.random.fold_in(_tk, 500 + 2), (1250, 128), jnp.float32)
        tbl_3 = 0.05 * jax.random.normal(jax.random.fold_in(_tk, 500 + 3), (1250, 128), jnp.float32)
        tbl_4 = 0.05 * jax.random.normal(jax.random.fold_in(_tk, 500 + 4), (1250, 128), jnp.float32)
        tbl_5 = 0.05 * jax.random.normal(jax.random.fold_in(_tk, 500 + 5), (1250, 128), jnp.float32)
        tbl_6 = 0.05 * jax.random.normal(jax.random.fold_in(_tk, 500 + 6), (12500, 128), jnp.float32)
        tbl_7 = 0.05 * jax.random.normal(jax.random.fold_in(_tk, 500 + 7), (1250, 128), jnp.float32)
        tbl_8 = 0.05 * jax.random.normal(jax.random.fold_in(_tk, 500 + 8), (12500, 128), jnp.float32)
        tbl_9 = 0.05 * jax.random.normal(jax.random.fold_in(_tk, 500 + 9), (12500, 128), jnp.float32)
        tbl_10 = 0.05 * jax.random.normal(jax.random.fold_in(_tk, 500 + 10), (125000, 128), jnp.float32)
        tbl_11 = 0.05 * jax.random.normal(jax.random.fold_in(_tk, 500 + 11), (12500, 128), jnp.float32)
        tbl_12 = 0.05 * jax.random.normal(jax.random.fold_in(_tk, 500 + 12), (1250, 128), jnp.float32)
        tbl_13 = 0.05 * jax.random.normal(jax.random.fold_in(_tk, 500 + 13), (1250, 128), jnp.float32)
        tbl_14 = 0.05 * jax.random.normal(jax.random.fold_in(_tk, 500 + 14), (1250, 128), jnp.float32)
        tbl_15 = 0.05 * jax.random.normal(jax.random.fold_in(_tk, 500 + 15), (12500, 128), jnp.float32)
        tbl_16 = 0.05 * jax.random.normal(jax.random.fold_in(_tk, 500 + 16), (1250, 128), jnp.float32)
        tbl_17 = 0.05 * jax.random.normal(jax.random.fold_in(_tk, 500 + 17), (12500, 128), jnp.float32)
        tbl_18 = 0.05 * jax.random.normal(jax.random.fold_in(_tk, 500 + 18), (12500, 128), jnp.float32)
        tbl_19 = 0.05 * jax.random.normal(jax.random.fold_in(_tk, 500 + 19), (1250, 128), jnp.float32)
        tbl_20 = 0.05 * jax.random.normal(jax.random.fold_in(_tk, 500 + 20), (1000, 128), jnp.float32)
        tbl_21 = 0.05 * jax.random.normal(jax.random.fold_in(_tk, 500 + 21), (1000, 128), jnp.float32)
        tbl_22 = 0.05 * jax.random.normal(jax.random.fold_in(_tk, 500 + 22), (12500, 128), jnp.float32)
        tbl_23 = 0.05 * jax.random.normal(jax.random.fold_in(_tk, 500 + 23), (1250, 128), jnp.float32)
        tbl_24 = 0.05 * jax.random.normal(jax.random.fold_in(_tk, 500 + 24), (1250, 128), jnp.float32)
        tbl_25 = 0.05 * jax.random.normal(jax.random.fold_in(_tk, 500 + 25), (1000, 128), jnp.float32)
        _rk = jax.random.fold_in(_tk, 7)
        r_bottom_output = -0.000520686 + 1.00062 * jax.random.normal(jax.random.fold_in(_rk, 101), (2048, 128), jnp.float32)
        W_top1 = 0.0456912 * jax.random.normal(jax.random.fold_in(_tk, 801), (479, 512), jnp.float32)
        W_top2 = 0.0441942 * jax.random.normal(jax.random.fold_in(_tk, 802), (512, 256), jnp.float32)
        W_top3 = 0.0625 * jax.random.normal(jax.random.fold_in(_tk, 803), (256, 1), jnp.float32)
        b_top1 = jnp.zeros((512,), jnp.float32)
        b_top2 = jnp.zeros((256,), jnp.float32)
        return (r_bottom_output, ids, tbl_0, tbl_1, tbl_2, tbl_3, tbl_4, tbl_5, tbl_6, tbl_7, tbl_8, tbl_9, tbl_10, tbl_11, tbl_12, tbl_13, tbl_14, tbl_15, tbl_16, tbl_17, tbl_18, tbl_19, tbl_20, tbl_21, tbl_22, tbl_23, tbl_24, tbl_25, W_top1, b_top1, W_top2, b_top2, W_top3)
    r_bottom_output, ids, tbl_0, tbl_1, tbl_2, tbl_3, tbl_4, tbl_5, tbl_6, tbl_7, tbl_8, tbl_9, tbl_10, tbl_11, tbl_12, tbl_13, tbl_14, tbl_15, tbl_16, tbl_17, tbl_18, tbl_19, tbl_20, tbl_21, tbl_22, tbl_23, tbl_24, tbl_25, W_top1, b_top1, W_top2, b_top2, W_top3 = _rec_inputs()

    def _L0_rec_setup():
        import jax, jax.numpy as jnp
        import numpy as np
        NUM_FEATURES = 27
        _TRIU_I, _TRIU_J = np.triu_indices(NUM_FEATURES, k=1)
        key = jax.random.key(seed)
        k1, k2 = jax.random.split(key)
        bottom_output = jax.random.normal(k1, (2048, 128), dtype=jnp.float32)
        embeddings = jax.random.normal(k2, (2048, 26, 128), dtype=jnp.float32)
        return {'bottom_output': bottom_output, 'embeddings': embeddings}
    _L0_rec_all = _L0_rec_setup()
    _L0_rec_in = {k: v for k, v in _L0_rec_all.items() if k in ()}
    del _L0_rec_all
    return {'r_bottom_output': r_bottom_output, 'ids': ids, 'tbl_0': tbl_0, 'tbl_1': tbl_1, 'tbl_2': tbl_2, 'tbl_3': tbl_3, 'tbl_4': tbl_4, 'tbl_5': tbl_5, 'tbl_6': tbl_6, 'tbl_7': tbl_7, 'tbl_8': tbl_8, 'tbl_9': tbl_9, 'tbl_10': tbl_10, 'tbl_11': tbl_11, 'tbl_12': tbl_12, 'tbl_13': tbl_13, 'tbl_14': tbl_14, 'tbl_15': tbl_15, 'tbl_16': tbl_16, 'tbl_17': tbl_17, 'tbl_18': tbl_18, 'tbl_19': tbl_19, 'tbl_20': tbl_20, 'tbl_21': tbl_21, 'tbl_22': tbl_22, 'tbl_23': tbl_23, 'tbl_24': tbl_24, 'tbl_25': tbl_25, 'W_top1': W_top1, 'b_top1': b_top1, 'W_top2': W_top2, 'b_top2': b_top2, 'W_top3': W_top3}

def reference(r_bottom_output, ids, tbl_0, tbl_1, tbl_2, tbl_3, tbl_4, tbl_5, tbl_6, tbl_7, tbl_8, tbl_9, tbl_10, tbl_11, tbl_12, tbl_13, tbl_14, tbl_15, tbl_16, tbl_17, tbl_18, tbl_19, tbl_20, tbl_21, tbl_22, tbl_23, tbl_24, tbl_25, W_top1, b_top1, W_top2, b_top2, W_top3):
    import jax
    import jax.numpy as jnp

    def _L0_rec_ref(bottom_output, embeddings):
        import jax, jax.numpy as jnp
        import numpy as np
        NUM_FEATURES = 27
        _TRIU_I, _TRIU_J = np.triu_indices(NUM_FEATURES, k=1)
        all_emb = jnp.concatenate([bottom_output[:, None, :], embeddings], axis=1)
        gram = jnp.einsum('bfd,bgd->bfg', all_emb, all_emb)
        return gram[:, _TRIU_I, _TRIU_J]
    e = jnp.stack([tbl_0[ids[:, 0]], tbl_1[ids[:, 1]], tbl_2[ids[:, 2]], tbl_3[ids[:, 3]], tbl_4[ids[:, 4]], tbl_5[ids[:, 5]], tbl_6[ids[:, 6]], tbl_7[ids[:, 7]], tbl_8[ids[:, 8]], tbl_9[ids[:, 9]], tbl_10[ids[:, 10]], tbl_11[ids[:, 11]], tbl_12[ids[:, 12]], tbl_13[ids[:, 13]], tbl_14[ids[:, 14]], tbl_15[ids[:, 15]], tbl_16[ids[:, 16]], tbl_17[ids[:, 17]], tbl_18[ids[:, 18]], tbl_19[ids[:, 19]], tbl_20[ids[:, 20]], tbl_21[ids[:, 21]], tbl_22[ids[:, 22]], tbl_23[ids[:, 23]], tbl_24[ids[:, 24]], tbl_25[ids[:, 25]]], axis=1)
    z = _L0_rec_ref(r_bottom_output, e)
    z = z.reshape(z.shape[0], -1)
    h = jnp.concatenate([z, r_bottom_output], axis=1)
    h = jnp.maximum(h @ W_top1 + b_top1, 0.0)
    h = jnp.maximum(h @ W_top2 + b_top2, 0.0)
    y = h @ W_top3
    return y

_drawn_inputs = setup_inputs


def setup_inputs(seed=0):
    import zlib

    import numpy as np

    out = dict(_drawn_inputs(seed))
    spreads = {'b_top1': (0.0, 0.1), 'b_top2': (0.0, 0.1)}
    factors = {}
    for name, (base, spread) in spreads.items():
        noise = np.random.default_rng([zlib.crc32(name.encode()), seed]).standard_normal(out[name].shape)
        drawn = base * np.exp(spread * noise) if base else spread * noise
        out[name] = jnp.asarray(drawn.astype(out[name].dtype))
    for name, factor in factors.items():
        out[name] = (out[name] * factor).astype(out[name].dtype)
    return out
```

```python
import concourse.bass as bass
from concourse import mybir
from contextlib import ExitStack

BATCH = 2048
D = 128
N_TABLES = 26
N_FEAT = N_TABLES + 1
P = 128
TILES = BATCH // P
PAIR = 2
STEPS = TILES // PAIR
MB = PAIR * P
ROWS_PER_BLOCK = 125
ONE_HOT = {0: 1000, 20: 1000, 21: 1000, 25: 1000, 1: 1250, 2: 1250}
OH = list(ONE_HOT)
OH_BLOCKS = [ONE_HOT[f] // ROWS_PER_BLOCK for f in OH]
MAX_BLOCKS = max(OH_BLOCKS)
BLOCK_KINDS = sorted(set(OH_BLOCKS))
GATHERED = [f for f in range(N_TABLES) if f not in ONE_HOT]
SLOTS = [-1] + GATHERED + OH
N_ROWS = 1 + len(GATHERED)
GROUP = 4
GROUPS = -(-N_ROWS // GROUP)
FPAD = 28
QUAD = 32
HALF = N_FEAT // 2
ROWS_PER_K = 9
KT = N_FEAT // ROWS_PER_K
KP = ROWS_PER_K * HALF
TROW = N_FEAT + HALF
H1, H2 = 512, 256
NT1, NT2 = H1 // P, H2 // P

AHEAD = [("A", 0), ("A", 1)]
RING = ([("T", 0, 0), ("T", 0, 1), ("A", 2), ("T", 0, 2), ("A", 3), ("T", 0, 3), ("A", 4), ("T", 0, 4), ("A", 5)]
        + [("T", 0, j) for j in range(5, GROUPS)]
        + [("T", 1, j) for j in range(GROUPS)] + [("P", 0), ("A", 0), ("P", 1), ("A", 1)])
ENTRIES = len(RING)
BANKS = 3
assert len(RING) == PAIR * GROUPS + PAIR + len(OH) and RING.index(("P", 1)) == RING.index(AHEAD[0]) + 1


def group_features(j):
    return range(j * GROUP, min((j + 1) * GROUP, N_ROWS))


def group_gathers(j):
    return [f for f in group_features(j) if f > 0]


def bank_of(entry):
    return RING.index(entry) % BANKS


def filled(step, entry, last=False):
    if last and entry == ("P", 1):
        return filled(step, entry) - 1
    if isinstance(step, int) and step == 0 and entry in AHEAD:
        return AHEAD.index(entry) + 1
    body = step - 1 if entry in AHEAD else step
    return len(AHEAD) + ENTRIES * body + RING.index(entry) + 1


def freed(body, entry):
    i = RING.index(entry)
    before = i - BANKS
    if before < 0:
        if isinstance(body, int) and body == 0:
            return max([n + 1 for n, e in enumerate(AHEAD) if bank_of(e) == i], default=0)
        before = max(k for k in range(ENTRIES) if k % BANKS == i) - ENTRIES
    return len(AHEAD) + ENTRIES * body + before + 1


def dlrm_tower(nc, bottom, ids, oh_ids, tables, oh_tables, row_ids, w1_pairs, w1_bottom, b1, w2, b2, w3, y):
    fp32, fp32r = mybir.dt.float32, mybir.dt.float32r
    ACT = mybir.ActivationFunctionType
    ALU = mybir.AluOpType
    ctx = ExitStack()
    with ctx:
        def sb(name, shape, dt=fp32):
            return ctx.enter_context(nc.sbuf_tensor(name, shape, dt))

        def ps(name, shape):
            return ctx.enter_context(nc.psum_tensor(name, shape, fp32))

        def sem(name):
            return ctx.enter_context(nc.semaphore(name))

        NG = len(GATHERED)
        ids_sb = sb("ids_sb", [P, PAIR, NG], mybir.dt.uint32)
        emb = sb("emb", [P, PAIR, N_ROWS, D])
        embT = sb("embT", [D, PAIR, P, FPAD])
        gramT = sb("gramT", [P, PAIR, N_FEAT + 1, TROW])
        pairs = sb("pairs", [P, PAIR, KT * KP])
        pairsT = sb("pairsT", [KP, KT, PAIR, P])
        w1z_sb = sb("w1z_sb", [KP, KT, H1])
        w1b_sb = sb("w1b_sb", [D, H1])
        w2_sb = sb("w2_sb", [P, NT1, H2])
        w3_sb = sb("w3_sb", [P, NT2])
        b1_sb = sb("b1_sb", [P, NT1])
        b2_sb = sb("b2_sb", [P, NT2])
        h1_sb = sb("h1_sb", [P, NT1, MB])
        h2_sb = sb("h2_sb", [P, NT2, MB])
        y_sb = sb("y_sb", [1, STEPS, MB])
        ident = sb("ident", [P, P])
        oh_ids_sb = sb("oh_ids_sb", [len(OH), STEPS, MB], mybir.dt.int32)
        oh_ids_f = sb("oh_ids_f", [len(OH), STEPS, MB], fp32r)
        pick = sb("pick", [len(OH), len(OH), ROWS_PER_BLOCK], fp32r)
        row_ids_sb = sb("row_ids_sb", [ROWS_PER_BLOCK, len(BLOCK_KINDS), MAX_BLOCKS])
        staged = [sb(f"staged{i}", [ROWS_PER_BLOCK, MAX_BLOCKS, D]) for i in range(2)]
        table_hi = sb("table_hi", [ROWS_PER_BLOCK, len(OH), MAX_BLOCKS, D], fp32r)
        table_lo = sb("table_lo", [ROWS_PER_BLOCK, len(OH), MAX_BLOCKS, D], fp32r)
        onehot = [sb(f"onehot{i}", [ROWS_PER_BLOCK, MAX_BLOCKS, MB], fp32r) for i in range(2)]

        ring = [ps(f"ring{i}", [P, GROUP, P]) for i in range(BANKS)]
        gram_ps = ps("gram_ps", [P, QUAD, QUAD])
        id_ps = ps("id_ps", [P, 512])
        mlp_ps = [ps(f"mlp_ps{i}", [P, 512]) for i in range(2)]

        s_ids = [sem(f"ids_loaded_{s}") for s in range(PAIR)]
        s_bot = [sem(f"bottom_loaded_{s}") for s in range(PAIR)]
        s_const = sem("row_ids_loaded")
        s_tab = [sem(f"table_staged_{i}") for i in range(2)]
        s_w = sem("weights_loaded")
        s_id0 = sem("ident_zeroed")
        s_ident = sem("ident_ready")
        s_gz = sem("gram_psum_zeroed")
        s_emb = [[sem(f"gathered_{s}_{j}") for j in range(GROUPS)] for s in range(PAIR)]
        s_pick = sem("pick_and_ids_ready")
        s_hi = sem("table_hi_ready")
        s_lo = sem("table_lo_ready")
        s_bc = sem("ids_broadcast")
        s_oh = sem("onehot_ready")
        s_fill = sem("ring_filled")
        s_free = sem("ring_copied_out")
        s_gram = sem("gram_done")
        s_gT = sem("gram_transposed")
        s_wrap = sem("gram_wrapped")
        s_pack = sem("pairs_packed")
        s_m1 = sem("h1_products")
        s_h1 = sem("h1_ready")
        s_m2 = sem("h2_products")
        s_h2 = sem("h2_ready")
        s_m3 = sem("y_product")
        s_y = sem("y_ready")
        s_out = sem("y_stored")

        def nth(step, m):
            return len(OH) * step + m + 1

        block = ctx.enter_context(nc.Block())

        @block.sync
        def _(sp):
            def load_tile(step, slot):
                t = step * PAIR + slot
                sp.dma_start(ids_sb[:, slot, :], ids[:, bass.ds(t, 1), :].rearrange("p t f -> p (t f)")).then_inc(s_ids[slot], 16)
                sp.dma_start(emb[:, slot, 0, :], bottom[bass.ds(t * P, P), :]).then_inc(s_bot[slot], 16)

            load_tile(0, 0)
            sp.dma_start(oh_ids_sb[:, :, :], oh_ids).then_inc(s_const, 16)
            sp.dma_start(row_ids_sb[:, :, :], row_ids).then_inc(s_const, 16)
            for m, n in enumerate(OH_BLOCKS):
                if m >= 2:
                    sp.wait_ge(s_hi, m - 1)
                    sp.wait_ge(s_lo, m - 1)
                sp.dma_start(staged[m % 2][:, 0:n, :], oh_tables[m].rearrange("(p n) d -> p n d", n=n)).then_inc(s_tab[m % 2], 16)
                if m == 0:
                    load_tile(0, 1)
            sp.dma_start(w1z_sb[:, :, :], w1_pairs.rearrange("(k p) n -> p k n", p=KP)).then_inc(s_w, 16)
            sp.dma_start(w1b_sb[:, :], w1_bottom).then_inc(s_w, 16)
            sp.dma_start(w2_sb[:, :, :], w2.rearrange("(k p) n -> p k n", p=P)).then_inc(s_w, 16)
            sp.dma_start(w3_sb[:, :], w3).then_inc(s_w, 16)
            sp.dma_start(b1_sb[:, :], b1).then_inc(s_w, 16)
            sp.dma_start(b2_sb[:, :], b2).then_inc(s_w, 16)
            with sp.Fori(1, STEPS) as step:
                for slot in range(PAIR):
                    sp.wait_ge(s_fill, filled(step - 1, ("T", slot, GROUPS - 1)))
                    load_tile(step, slot)
            sp.wait_ge(s_y, STEPS)
            sp.dma_start(y.rearrange("b o -> o b"), y_sb[:, :, :].rearrange("o s m -> o (s m)")).then_inc(s_out, 16)
            sp.wait_ge(s_out, 16)

        @block.gpsimd
        def _(pool):
            pool.memset(ident[:, :], 0.0).then_inc(s_id0, 1)
            pool.wait_ge(s_id0, 1)
            pool.affine_select(out=ident[:, :], in_=ident[:, :], compare_op=ALU.not_equal, fill=1.0,
                               base=0, pattern=[[-1, P]], channel_multiplier=1).then_inc(s_ident, 1)

            def gather(step, slot, wait):
                pool.wait_ge(s_ids[slot], 16 * (step + 1))
                for j in range(GROUPS):
                    if wait:
                        pool.wait_ge(s_fill, filled(step - 1, ("T", slot, j)))
                        pool.nop(nofuse=True)
                    for f in group_gathers(j):
                        pool.indirect_dma_start(
                            out=emb[:, slot, f, :], out_offset=None, in_=tables[f - 1],
                            in_offset=bass.IndirectOffsetOnAxis(ap=ids_sb[:, slot, f - 1:f], axis=0),
                        ).then_inc(s_emb[slot][j], 16)

            for slot in range(PAIR):
                gather(0, slot, False)
            with pool.Fori(1, STEPS) as step:
                for slot in range(PAIR):
                    gather(step, slot, True)

        @block.tensor
        def _(pe):
            def wait_bank(body, entry):
                n = freed(body, entry)
                if not (isinstance(n, int) and n == 0):
                    pe.wait_ge(s_free, n)

            def broadcast_ids(step, m):
                if not (isinstance(step, int) and nth(step, m) == 1):
                    pe.wait_ge(s_oh, nth(step, m) - 1)
                    pe.nop(nofuse=True)
                pe.matmul(id_ps[0:ROWS_PER_BLOCK, 0:MB], pick[:, m, :],
                          oh_ids_f[:, bass.ds(step, 1), :].rearrange("f s m -> f (s m)"),
                          start=True, stop=True).then_inc(s_bc, 1)

            def read_table(step, body, m, first=False):
                entry = ("A", m)
                pe.wait_ge(s_oh, nth(step, m))
                if first:
                    pe.wait_ge(s_lo, m + 1)
                    pe.wait_ge(s_hi, m + 1)
                if body is not None:
                    wait_bank(body, entry)
                out = ring[bank_of(entry)][:, 0:PAIR, :].rearrange("p s b -> p (s b)")
                n = OH_BLOCKS[m]
                for b in range(n):
                    for part in (table_hi, table_lo):
                        last = pe.matmul(out, part[:, m, b, :], onehot[m % 2][:, b, :],
                                         start=(b == 0 and part is table_hi), stop=(b == n - 1 and part is table_lo))
                last.then_inc(s_fill, 1)

            def transpose_group(step, slot, j, first):
                entry = ("T", slot, j)
                if j == 0:
                    pe.wait_ge(s_bot[slot], 16 * (step + 1))
                pe.wait_ge(s_emb[slot][j], 16 * len(group_gathers(j)) * (step + 1))
                wait_bank(step, entry)
                for i, f in enumerate(group_features(j)):
                    last = pe.transpose(ring[bank_of(entry)][:, i, :], emb[:, slot, f, :], ident[:, :])
                last.then_inc(s_fill, 1)

            def gram(step, slot, first):
                last_in = RING.index(("T", slot, GROUPS - 1)) if slot else max(RING.index(("T", 0, GROUPS - 1)), RING.index(("A", 5)))
                pe.wait_ge(s_free, len(AHEAD) + ENTRIES * step + last_in + 1)
                if first and slot == 0:
                    pe.wait_ge(s_gz, 1)
                else:
                    pe.wait_ge(s_gT, step * PAIR + slot)
                for q in range(QUAD):
                    for s in range(P // QUAD):
                        e = embT[:, slot, s * QUAD + q, 0:N_FEAT]
                        last = pe.matmul(gram_ps[s * QUAD:s * QUAD + N_FEAT, q, 0:N_FEAT], e, e,
                                         start=True, stop=True)
                last.then_inc(s_gram, 1)

            def transpose_pairs(step, slot):
                entry = ("P", slot)
                pe.wait_ge(s_pack, step * PAIR + slot + 1)
                wait_bank(step, entry)
                for k in range(KT):
                    last = pe.transpose(ring[bank_of(entry)][0:KP, k, :], pairs[:, slot, k * KP:(k + 1) * KP], ident[:, :])
                last.then_inc(s_fill, 1)

            def h1_products(step, first, last):
                pe.wait_ge(s_free, filled(step, ("P", 1), last))
                if first:
                    pe.wait_ge(s_w, 16 * 6)
                else:
                    pe.wait_ge(s_y, step)
                for n in range(NT1):
                    if n >= 2:
                        pe.wait_ge(s_h1, step * NT1 + n - 1)
                    out = mlp_ps[n % 2][:, 0:MB]
                    for k in range(KT):
                        pe.matmul(out, w1z_sb[:, k, n * P:(n + 1) * P],
                                  pairsT[:, k, :, :].rearrange("p s b -> p (s b)"), start=(k == 0), stop=False)
                    pe.matmul(out, w1b_sb[:, n * P:(n + 1) * P], embT[:, :, :, 0],
                              start=False, stop=True).then_inc(s_m1, 1)

            def h2_and_y_products(step):
                pe.wait_ge(s_h1, (step + 1) * NT1)
                for n in range(NT2):
                    for k in range(NT1):
                        last = pe.matmul(mlp_ps[n][:, 0:MB], w2_sb[:, k, n * P:(n + 1) * P], h1_sb[:, k, :],
                                         start=(k == 0), stop=(k == NT1 - 1))
                    last.then_inc(s_m2, 1)
                pe.wait_ge(s_h2, (step + 1) * NT2)
                for k in range(NT2):
                    last = pe.matmul(mlp_ps[0][0:1, 0:MB], w3_sb[:, k:k + 1], h2_sb[:, k, :],
                                     start=(k == 0), stop=(k == NT2 - 1))
                last.then_inc(s_m3, 1)

            def step_of(step, first, last):
                for entry in RING[0:RING.index(("P", 0))]:
                    if entry[0] == "A":
                        m = entry[1]
                        if m + 1 < len(OH):
                            broadcast_ids(step, m + 1)
                        read_table(step, step, m, first)
                        if m + 1 == len(OH) and not last:
                            broadcast_ids(step + 1, 0)
                    else:
                        if entry == ("T", 1, 0):
                            gram(step, 0, first)
                        transpose_group(step, entry[1], entry[2], first)
                transpose_pairs(step, 0)
                gram(step, 1, first)
                if not last:
                    broadcast_ids(step + 1, 1)
                    read_table(step + 1, step, 0)
                transpose_pairs(step, 1)
                h1_products(step, first, last)
                if not last:
                    broadcast_ids(step + 1, 2)
                    read_table(step + 1, step, 1)
                h2_and_y_products(step)

            pe.wait_ge(s_pick, 2)
            pe.wait_ge(s_ident, 1)
            broadcast_ids(0, 0)
            broadcast_ids(0, 1)
            read_table(0, None, 0, True)
            broadcast_ids(0, 2)
            read_table(0, None, 1, True)
            step_of(0, True, False)
            with pe.Fori(1, STEPS - 1) as step:
                step_of(step, False, False)
            step_of(STEPS - 1, False, True)

        @block.scalar
        def _(act):
            def copy_out(step, entry, last=False):
                act.wait_ge(s_fill, filled(step, entry, last))
                bank = ring[bank_of(entry)]
                if entry[0] == "A":
                    out, src = embT[:, :, :, N_ROWS + entry[1]], bank[:, 0:PAIR, :]
                elif entry[0] == "T":
                    n = len(group_features(entry[2]))
                    at = entry[2] * GROUP
                    out, src = embT[:, entry[1], :, at:at + n], bank[:, 0:n, :].rearrange("p f b -> p b f")
                else:
                    out, src = pairsT[:, :, entry[1], :], bank[0:KP, 0:KT, :]
                nc.scalar.copy(out, src).then_inc(s_free, 1)

            def pack_pairs(step, slot):
                t = step * PAIR + slot
                act.wait_ge(s_gT, t + 1)
                nc.scalar.copy(gramT[:, slot, HALF + 1:N_FEAT, N_FEAT:TROW],
                               gramT[:, slot, HALF + 1:N_FEAT, 0:HALF]).then_inc(s_wrap, 1)
                act.wait_ge(s_wrap, t + 1)
                skew = gramT[:, slot, :, :].rearrange("p g f -> p (g f)")[:, 1:1 + N_FEAT * (TROW + 1)]
                nc.scalar.copy(pairs[:, slot, :].rearrange("p (g c) -> p g c", c=HALF),
                               skew.rearrange("p (g c) -> p g c", c=TROW + 1)[:, :, 0:HALF]).then_inc(s_pack, 1)

            def step_of(step, first, last):
                for entry in RING[0:RING.index(("P", 0))]:
                    copy_out(step, entry)
                    if entry == ("T", 1, 1):
                        pack_pairs(step, 0)
                copy_out(step, ("P", 0))
                pack_pairs(step, 1)
                if not last:
                    copy_out(step + 1, ("A", 0))
                copy_out(step, ("P", 1), last)
                for n in range(NT1):
                    act.wait_ge(s_m1, step * NT1 + n + 1)
                    nc.scalar.activation(h1_sb[:, n, :], mlp_ps[n % 2][:, 0:MB], ACT.Relu,
                                         bias=b1_sb[:, n:n + 1]).then_inc(s_h1, 1)
                if not last:
                    copy_out(step + 1, ("A", 1))
                for n in range(NT2):
                    act.wait_ge(s_m2, step * NT2 + n + 1)
                    nc.scalar.activation(h2_sb[:, n, :], mlp_ps[n][:, 0:MB], ACT.Relu,
                                         bias=b2_sb[:, n:n + 1]).then_inc(s_h2, 1)
                act.wait_ge(s_m3, step + 1)
                nc.scalar.copy(y_sb[:, bass.ds(step, 1), :].rearrange("o s m -> o (s m)"),
                               mlp_ps[0][0:1, 0:MB]).then_inc(s_y, 1)

            for m, n in enumerate(OH_BLOCKS):
                act.wait_ge(s_tab[m % 2], 16 * (m // 2 + 1))
                nc.scalar.copy(table_hi[:, m, 0:n, :], staged[m % 2][:, 0:n, :]).then_inc(s_hi, 1)
                if m == 1:
                    copy_out(0, ("A", 0))
                if m == 2:
                    copy_out(0, ("A", 1))
            act.wait_ge(s_w, 16 * 6)
            step_of(0, True, False)
            with act.Fori(1, STEPS - 1) as step:
                step_of(step, False, False)
            step_of(STEPS - 1, False, True)

        @block.vector
        def _(dve):
            def make_onehot(step, m, first=False):
                n = OH_BLOCKS[m]
                dve.wait_ge(s_bc, nth(step, m))
                if not (first and m < 2):
                    before = (step, m - 2) if m >= 2 else (step - 1, m - 2 + len(OH))
                    dve.wait_ge(s_fill, filled(before[0], ("A", before[1])))
                rows = row_ids_sb[:, BLOCK_KINDS.index(n), 0:n]
                nc.vector.tensor_tensor(
                    out=onehot[m % 2][:, 0:n, :],
                    in0=id_ps[0:ROWS_PER_BLOCK, 0:MB].unsqueeze(1).to_broadcast([ROWS_PER_BLOCK, n, MB]),
                    in1=rows.unsqueeze(2).to_broadcast([ROWS_PER_BLOCK, n, MB]),
                    op=ALU.is_equal).then_inc(s_oh, 1)

            def transpose_gram(step, slot):
                t = step * PAIR + slot
                dve.wait_ge(s_gram, t + 1)
                nc.vector.transpose(gramT[:, slot, 0:N_FEAT, 0:QUAD],
                                    gram_ps[:, :, 0:N_FEAT].rearrange("p q g -> p g q")).then_inc(s_gT, 1)

            def step_of(step, first, last):
                for m in range(3, len(OH)):
                    make_onehot(step, m, first)
                if not last:
                    make_onehot(step + 1, 0)
                transpose_gram(step, 0)
                transpose_gram(step, 1)
                if not last:
                    make_onehot(step + 1, 1)
                    make_onehot(step + 1, 2)

            def split_lo(m):
                n = OH_BLOCKS[m]
                dve.wait_ge(s_tab[m % 2], 16 * (m // 2 + 1))
                dve.wait_ge(s_hi, m + 1)
                nc.vector.tensor_tensor(out=table_lo[:, m, 0:n, :], in0=staged[m % 2][:, 0:n, :],
                                        in1=table_hi[:, m, 0:n, :].bitcast(fp32), op=ALU.subtract).then_inc(s_lo, 1)

            nc.vector.memset(gram_ps[:, :, :], 0.0).then_inc(s_gz, 1)
            dve.wait_ge(s_ident, 1)
            nc.vector.tensor_copy(pick[:, :, :], ident[0:len(OH), 0:len(OH)].unsqueeze(2).to_broadcast(
                [len(OH), len(OH), ROWS_PER_BLOCK])).then_inc(s_pick, 1)
            dve.wait_ge(s_const, 32)
            nc.vector.tensor_copy(oh_ids_f[:, :, :], oh_ids_sb[:, :, :]).then_inc(s_pick, 1)
            for m in range(3):
                make_onehot(0, m, True)
                split_lo(m)
            for m in range(3, len(OH)):
                split_lo(m)
            step_of(0, True, False)
            with dve.Fori(1, STEPS - 1) as step:
                step_of(step, False, False)
            step_of(STEPS - 1, False, True)


def kernel(**inputs):
    import numpy as np
    import concourse.bacc as bacc
    from concourse import mybir as mb
    from concourse.bass_utils import run_bass_kernel_spmd as run

    nc = bacc.Bacc("TRN2", target_bir_lowering=False, num_devices=1)
    arrays = {}

    def dram_in(name, a):
        a = np.ascontiguousarray(a)
        arrays[name] = a
        return nc.dram_tensor(name, a.shape, mb.dt.from_np(a.dtype), kind="ExternalInput").ap()

    n_pairs = N_FEAT * HALF
    pair_row = {pair: i for i, pair in enumerate(zip(*(v.tolist() for v in np.triu_indices(N_FEAT, k=1))))}
    feature = [f + 1 for f in SLOTS]
    order = np.array([pair_row[tuple(sorted((feature[g], feature[(g + 1 + c) % N_FEAT])))]
                      for g in range(N_FEAT) for c in range(HALF)])
    row_ids = np.zeros((ROWS_PER_BLOCK, len(BLOCK_KINDS), MAX_BLOCKS), np.float32)
    for i, n in enumerate(BLOCK_KINDS):
        row_ids[:, i, :n] = np.arange(ROWS_PER_BLOCK * n).reshape(ROWS_PER_BLOCK, n)
    w1 = np.asarray(inputs["W_top1"])
    ids = np.asarray(inputs["ids"])
    args = [
        dram_in("bottom", inputs["r_bottom_output"]),
        dram_in("ids", ids[:, GATHERED].view(np.uint32).reshape(TILES, P, len(GATHERED)).transpose(1, 0, 2)),
        dram_in("oh_ids", ids[:, OH].T.reshape(len(OH), STEPS, MB)),
        [dram_in(f"tbl_{f}", inputs[f"tbl_{f}"]) for f in GATHERED],
        [dram_in(f"tbl_{f}", inputs[f"tbl_{f}"]) for f in OH],
        dram_in("row_ids", row_ids),
        dram_in("w1_pairs", w1[order]),
        dram_in("w1_bottom", w1[n_pairs:]),
        dram_in("b1", np.asarray(inputs["b_top1"]).reshape(NT1, P).T),
        dram_in("w2", inputs["W_top2"]),
        dram_in("b2", np.asarray(inputs["b_top2"]).reshape(NT2, P).T),
        dram_in("w3", np.asarray(inputs["W_top3"]).reshape(NT2, P).T),
    ]
    y = nc.dram_tensor("y", (BATCH, 1), mb.dt.float32, kind="ExternalOutput").ap()
    dlrm_tower(nc, *args, y)
    r = run(nc, [arrays], core_ids=[0])
    return r.results[0]["y"]
```

```python
import concourse.bass as bass
from concourse import mybir
from contextlib import ExitStack

BATCH = 2048
D = 128
N_TABLES = 26
N_FEAT = N_TABLES + 1
P = 128
TILES = BATCH // P
PAIR = 2
STEPS = TILES // PAIR
MB = PAIR * P
ROWS_PER_BLOCK = 125
ONE_HOT = {1: 1250, 2: 1250, 3: 1250, 0: 1000, 20: 1000, 21: 1000, 25: 1000}
OH = list(ONE_HOT)
OH_BLOCKS = [ONE_HOT[f] // ROWS_PER_BLOCK for f in OH]
MAX_BLOCKS = max(OH_BLOCKS)
OH_AT = [sum(OH_BLOCKS[:m]) for m in range(len(OH))]
STAGES = 4
BLOCK_KINDS = sorted(set(OH_BLOCKS))
GATHERED = [f for f in range(N_TABLES) if f not in ONE_HOT]
SLOTS = [-1] + GATHERED + OH
N_ROWS = 1 + len(GATHERED)
GROUP = 4
GROUPS = -(-N_ROWS // GROUP)
FPAD = 28
QUAD = 32
HALF = N_FEAT // 2
ROWS_PER_K = 9
KT = N_FEAT // ROWS_PER_K
KP = ROWS_PER_K * HALF
TROW = N_FEAT + HALF
H1, H2 = 512, 256
NT1, NT2 = H1 // P, H2 // P

AHEAD = [("A", m) for m in range(4)]
READ_AFTER = {1: [4], 3: [5], 4: [6]}
RING_T0 = [e for j in range(GROUPS) for e in [("T", 0, j)] + [("A", m) for m in READ_AFTER.get(j, [])]]
EARLY_T1 = GROUPS
RING = (RING_T0 + [("T", 1, j) for j in range(EARLY_T1)] + [("P", 0)]
        + [("T", 1, j) for j in range(EARLY_T1, GROUPS)] + AHEAD[:1] + [("P", 1)] + AHEAD[1:])
ENTRIES = len(RING)
BANKS = 3
BANK = [i % BANKS for i in range(ENTRIES)]
if ENTRIES % BANKS == 1:
    BANK[-1] = 1
PASSES = STEPS + 1
assert ENTRIES == PAIR * GROUPS + PAIR + len(OH)


def group_features(j):
    return range(j * GROUP, min((j + 1) * GROUP, N_ROWS))


def group_gathers(j):
    return [f for f in group_features(j) if f > 0]


def bank_of(entry):
    return BANK[RING.index(entry)]


def filled(step, entry, last=False):
    if last and entry == ("P", 1):
        return filled(step, entry) - 1
    if isinstance(step, int) and step == 0 and entry in AHEAD:
        return AHEAD.index(entry) + 1
    body = step - 1 if entry in AHEAD else step
    return len(AHEAD) + ENTRIES * body + RING.index(entry) + 1


def freed(body, entry):
    i = RING.index(entry)
    same = [k for k in range(ENTRIES) if BANK[k] == BANK[i]]
    if i > same[0]:
        before = same[same.index(i) - 1]
    elif isinstance(body, int) and body == 0:
        return max([n + 1 for n, e in enumerate(AHEAD) if bank_of(e) == BANK[i]], default=0)
    else:
        before = same[-1] - ENTRIES
    return len(AHEAD) + ENTRIES * body + before + 1


def dlrm_tower(nc, bottom, ids, oh_ids, tables, oh_tables, row_ids, w1_pairs, w1_bottom, b1, w2, b2, w3, y):
    fp32, fp32r = mybir.dt.float32, mybir.dt.float32r
    ACT = mybir.ActivationFunctionType
    ALU = mybir.AluOpType
    ctx = ExitStack()
    with ctx:
        def sb(name, shape, dt=fp32):
            return ctx.enter_context(nc.sbuf_tensor(name, shape, dt))

        def ps(name, shape):
            return ctx.enter_context(nc.psum_tensor(name, shape, fp32))

        def sem(name):
            return ctx.enter_context(nc.semaphore(name))

        NG = len(GATHERED)
        ids_sb = sb("ids_sb", [P, PAIR, NG], mybir.dt.uint32)
        emb = sb("emb", [P, PAIR, N_ROWS, D])
        embT = sb("embT", [D, PAIR, P, FPAD])
        gramT = sb("gramT", [P, PAIR, N_FEAT + 1, TROW])
        pairs = sb("pairs", [P, PAIR, KT * KP])
        pairsT = sb("pairsT", [KP, KT, PAIR, P])
        w1z_sb = sb("w1z_sb", [KP, KT, H1])
        w1b_sb = sb("w1b_sb", [D, H1])
        w2_sb = sb("w2_sb", [P, NT1, H2])
        w3_sb = sb("w3_sb", [P, NT2])
        b1_sb = sb("b1_sb", [P, NT1])
        b2_sb = sb("b2_sb", [P, NT2])
        h1_sb = sb("h1_sb", [P, NT1, MB])
        h2_sb = sb("h2_sb", [P, NT2, MB])
        y_sb = sb("y_sb", [1, STEPS, MB])
        ident = sb("ident", [P, P])
        oh_ids_sb = gramT[0:len(OH), :, :, :].rearrange("f s g c -> f (s g c)")[:, 0:BATCH].bitcast(mybir.dt.int32)
        oh_ids_f = sb("oh_ids_f", [len(OH), STEPS, MB], fp32r)
        pick = sb("pick", [len(OH), len(OH), ROWS_PER_BLOCK], fp32r)
        row_ids_sb = sb("row_ids_sb", [ROWS_PER_BLOCK, len(BLOCK_KINDS), MAX_BLOCKS])
        staged = [sb(f"staged{i}", [ROWS_PER_BLOCK, MAX_BLOCKS, D]) for i in range(STAGES)]
        table_hi = sb("table_hi", [ROWS_PER_BLOCK, sum(OH_BLOCKS), D], fp32r)
        table_lo = sb("table_lo", [ROWS_PER_BLOCK, sum(OH_BLOCKS), D], fp32r)
        onehot = [sb(f"onehot{i}", [ROWS_PER_BLOCK, MAX_BLOCKS, MB], fp32r) for i in range(2)]

        ring = [ps(f"ring{i}", [P, GROUP, P]) for i in range(BANKS)]
        gram_ps = ps("gram_ps", [P, QUAD, QUAD])
        id_ps = ps("id_ps", [P, 512])
        mlp_ps = [ps(f"mlp_ps{i}", [P, 512]) for i in range(2)]

        s_ids = [sem(f"ids_loaded_{s}") for s in range(PAIR)]
        s_bot = [sem(f"bottom_loaded_{s}") for s in range(PAIR)]
        s_const = sem("row_ids_loaded")
        s_tab = [sem(f"table_staged_{i}") for i in range(STAGES)]
        s_w = sem("weights_loaded")
        s_id0 = sem("ident_zeroed")
        s_ident = sem("ident_ready")
        s_gz = sem("gram_psum_zeroed")
        s_emb = [[sem(f"gathered_{s}_{j}") for j in range(GROUPS)] for s in range(PAIR)]
        s_pick = sem("pick_and_ids_ready")
        s_hi = sem("table_hi_ready")
        s_lo = sem("table_lo_ready")
        s_bc = sem("ids_broadcast")
        s_oh = sem("onehot_ready")
        s_fill = sem("ring_filled")
        s_free = sem("ring_copied_out")
        s_gram = sem("gram_done")
        s_gT = sem("gram_transposed")
        s_wrap = sem("gram_wrapped")
        s_pack = sem("pairs_packed")
        s_m1 = sem("h1_products")
        s_h1 = sem("h1_ready")
        s_m2 = sem("h2_products")
        s_h2 = sem("h2_ready")
        s_m3 = sem("y_product")
        s_y = sem("y_ready")
        s_out = sem("y_stored")

        def nth(step, m):
            return len(OH) * step + m + 1

        block = ctx.enter_context(nc.Block())

        @block.sync
        def _(sp):
            def load_tile(step, slot):
                t = step * PAIR + slot
                sp.dma_start(ids_sb[:, slot, :], ids[:, bass.ds(t, 1), :].rearrange("p t f -> p (t f)")).then_inc(s_ids[slot], 16)
                sp.dma_start(emb[:, slot, 0, :], bottom[bass.ds(t * P, P), :]).then_inc(s_bot[slot], 16)

            load_tile(0, 0)
            sp.dma_start(oh_ids_sb, oh_ids).then_inc(s_const, 16)
            sp.dma_start(row_ids_sb[:, :, :], row_ids).then_inc(s_const, 16)
            for m, n in enumerate(OH_BLOCKS):
                if m >= STAGES:
                    sp.wait_ge(s_hi, m - STAGES + 1)
                    sp.wait_ge(s_lo, m - STAGES + 1)
                sp.dma_start(staged[m % STAGES][:, 0:n, :], oh_tables[m].rearrange("(p n) d -> p n d", n=n)).then_inc(s_tab[m % STAGES], 16)
                if m == 0:
                    load_tile(0, 1)
            sp.dma_start(w1z_sb[:, :, :], w1_pairs.rearrange("(k p) n -> p k n", p=KP)).then_inc(s_w, 16)
            sp.dma_start(w1b_sb[:, :], w1_bottom).then_inc(s_w, 16)
            sp.dma_start(w2_sb[:, :, :], w2.rearrange("(k p) n -> p k n", p=P)).then_inc(s_w, 16)
            sp.dma_start(w3_sb[:, :], w3).then_inc(s_w, 16)
            sp.dma_start(b1_sb[:, :], b1).then_inc(s_w, 16)
            sp.dma_start(b2_sb[:, :], b2).then_inc(s_w, 16)
            with sp.Fori(1, STEPS) as step:
                for slot in range(PAIR):
                    sp.wait_ge(s_fill, filled(step - 1, ("T", slot, GROUPS - 1)))
                    load_tile(step, slot)
            sp.wait_ge(s_y, PASSES)
            sp.dma_start(y.rearrange("b o -> o b"), y_sb[:, :, :].rearrange("o s m -> o (s m)")).then_inc(s_out, 16)
            sp.wait_ge(s_out, 16)

        @block.gpsimd
        def _(pool):
            pool.memset(ident[:, :], 0.0).then_inc(s_id0, 1)
            pool.wait_ge(s_id0, 1)
            pool.affine_select(out=ident[:, :], in_=ident[:, :], compare_op=ALU.not_equal, fill=1.0,
                               base=0, pattern=[[-1, P]], channel_multiplier=1).then_inc(s_ident, 1)

            def gather(step, slot, wait):
                pool.wait_ge(s_ids[slot], 16 * (step + 1))
                for j in range(GROUPS):
                    if wait:
                        pool.wait_ge(s_fill, filled(step - 1, ("T", slot, j)))
                        pool.nop(nofuse=True)
                    for f in group_gathers(j):
                        pool.indirect_dma_start(
                            out=emb[:, slot, f, :], out_offset=None, in_=tables[f - 1],
                            in_offset=bass.IndirectOffsetOnAxis(ap=ids_sb[:, slot, f - 1:f], axis=0),
                        ).then_inc(s_emb[slot][j], 16)

            for slot in range(PAIR):
                gather(0, slot, False)
            with pool.Fori(1, STEPS) as step:
                for slot in range(PAIR):
                    gather(step, slot, True)

        @block.tensor
        def _(pe):
            def wait_bank(body, entry):
                n = freed(body, entry)
                if not (isinstance(n, int) and n == 0):
                    pe.wait_ge(s_free, n)

            def broadcast_ids(step, m):
                if not (isinstance(step, int) and nth(step, m) == 1):
                    pe.wait_ge(s_oh, nth(step, m) - 1)
                    pe.nop(nofuse=True)
                pe.matmul(id_ps[0:ROWS_PER_BLOCK, 0:MB], pick[:, m, :],
                          oh_ids_f[:, bass.ds(step, 1), :].rearrange("f s m -> f (s m)"),
                          start=True, stop=True).then_inc(s_bc, 1)

            def read_table(step, body, m, first=False):
                entry = ("A", m)
                pe.wait_ge(s_oh, nth(step, m))
                if first:
                    pe.wait_ge(s_lo, m + 1)
                    pe.wait_ge(s_hi, m + 1)
                if body is not None:
                    wait_bank(body, entry)
                out = ring[bank_of(entry)][:, 0:PAIR, :].rearrange("p s b -> p (s b)")
                n = OH_BLOCKS[m]
                for b in range(n):
                    for part in (table_hi, table_lo):
                        last = pe.matmul(out, part[:, OH_AT[m] + b, :], onehot[m % 2][:, b, :],
                                         start=(b == 0 and part is table_hi), stop=(b == n - 1 and part is table_lo))
                last.then_inc(s_fill, 1)

            def transpose_group(step, slot, j, first):
                entry = ("T", slot, j)
                if j == 0:
                    pe.wait_ge(s_bot[slot], 16 * (step + 1))
                pe.wait_ge(s_emb[slot][j], 16 * len(group_gathers(j)) * (step + 1))
                wait_bank(step, entry)
                for i, f in enumerate(group_features(j)):
                    last = pe.transpose(ring[bank_of(entry)][:, i, :], emb[:, slot, f, :], ident[:, :])
                last.then_inc(s_fill, 1)

            def gram(step, slot, first):
                pe.wait_ge(s_free, filled(step, RING_T0[-1] if slot == 0 else ("T", 1, GROUPS - 1)))
                if first and slot == 0:
                    pe.wait_ge(s_gz, 1)
                else:
                    pe.wait_ge(s_gT, step * PAIR + slot)
                for q in range(QUAD):
                    for s in range(P // QUAD):
                        e = embT[:, slot, s * QUAD + q, 0:N_FEAT]
                        last = pe.matmul(gram_ps[s * QUAD:s * QUAD + N_FEAT, q, 0:N_FEAT], e, e,
                                         start=True, stop=True)
                last.then_inc(s_gram, 1)

            def transpose_pairs(step, slot):
                entry = ("P", slot)
                pe.wait_ge(s_pack, step * PAIR + slot + 1)
                wait_bank(step, entry)
                for k in range(KT):
                    last = pe.transpose(ring[bank_of(entry)][0:KP, k, :], pairs[:, slot, k * KP:(k + 1) * KP], ident[:, :])
                last.then_inc(s_fill, 1)

            def h1_products(p, n, tiles, pairs_in=None):
                if n >= 2:
                    pe.wait_ge(s_h1, p * NT1 + n - 1)
                out = mlp_ps[n % 2][:, 0:P * len(tiles)]
                at = slice(tiles[0], tiles[-1] + 1)
                pe.matmul(out, w1b_sb[:, n * P:(n + 1) * P], embT[:, at, :, 0], start=True, stop=False)
                if n == 0:
                    pe.wait_ge(s_free, pairs_in)
                for k in range(KT):
                    last = pe.matmul(out, w1z_sb[:, k, n * P:(n + 1) * P],
                                     pairsT[:, k, at, :].rearrange("p s b -> p (s b)"), start=False, stop=(k == KT - 1))
                last.then_inc(s_m1, 1)

            def h2_products(p, n, tiles):
                for k in range(NT1):
                    if n == 0 and k == 0:
                        pe.wait_ge(s_h1, (p + 1) * NT1 - 1)
                    if n == 0 and k == NT1 - 1:
                        pe.wait_ge(s_h1, (p + 1) * NT1)
                    last = pe.matmul(mlp_ps[n][:, 0:P * len(tiles)], w2_sb[:, k, n * P:(n + 1) * P],
                                     h1_sb[:, k, 0:P * len(tiles)], start=(k == 0), stop=(k == NT1 - 1))
                last.then_inc(s_m2, 1)

            def y_product(p, tiles):
                for k in range(NT2):
                    pe.wait_ge(s_h2, p * NT2 + k + 1)
                    last = pe.matmul(mlp_ps[0][0:1, 0:P * len(tiles)], w3_sb[:, k:k + 1],
                                     h2_sb[:, k, 0:P * len(tiles)], start=(k == 0), stop=(k == NT2 - 1))
                last.then_inc(s_m3, 1)

            def read_ahead(step, m):
                broadcast_ids(step + 1, m + 1)
                read_table(step + 1, step, m)

            both = [0, 1]

            def first_tile(step, first, last):
                for entry in RING_T0:
                    if entry[0] == "T":
                        transpose_group(step, 0, entry[2], first)
                    else:
                        if entry[1] + 1 < len(OH):
                            broadcast_ids(step, entry[1] + 1)
                        read_table(step, step, entry[1], first)
                if not last:
                    broadcast_ids(step + 1, 0)
                if not first:
                    h2_products(step - 1, 0, both)
                gram(step, 0, first)

            def step_of(step, first):
                first_tile(step, first, False)
                for j in range(EARLY_T1):
                    transpose_group(step, 1, j, first)
                if not first:
                    h2_products(step - 1, 1, both)
                transpose_pairs(step, 0)
                for j in range(EARLY_T1, GROUPS):
                    transpose_group(step, 1, j, first)
                gram(step, 1, first)
                read_ahead(step, 0)
                transpose_pairs(step, 1)
                if not first:
                    y_product(step - 1, both)
                read_ahead(step, 1)
                if first:
                    pe.wait_ge(s_w, 16 * 6)
                else:
                    pe.wait_ge(s_y, step)
                h1_products(step, 0, both, filled(step, ("P", 1)))
                h1_products(step, 1, both)
                read_ahead(step, 2)
                h1_products(step, 2, both)
                h1_products(step, 3, both)
                read_ahead(step, 3)

            def last_step(step):
                first_tile(step, False, True)
                for j in range(EARLY_T1):
                    transpose_group(step, 1, j, False)
                h2_products(step - 1, 1, both)
                transpose_pairs(step, 0)
                y_product(step - 1, both)
                pe.wait_ge(s_y, step)
                for n in range(NT1):
                    h1_products(step, n, [0], filled(step, ("P", 0)))
                for j in range(EARLY_T1, GROUPS):
                    transpose_group(step, 1, j, False)
                h2_products(step, 0, [0])
                gram(step, 1, False)
                h2_products(step, 1, [0])
                y_product(step, [0])
                transpose_pairs(step, 1)
                pe.wait_ge(s_y, step + 1)
                for n in range(NT1):
                    h1_products(step + 1, n, [1], filled(step, ("P", 1), True))
                for n in range(NT2):
                    h2_products(step + 1, n, [1])
                y_product(step + 1, [1])

            pe.wait_ge(s_pick, 2)
            pe.wait_ge(s_ident, 1)
            broadcast_ids(0, 0)
            for m in range(len(AHEAD)):
                broadcast_ids(0, m + 1)
                read_table(0, None, m, True)
            step_of(0, True)
            with pe.Fori(1, STEPS - 1) as step:
                step_of(step, False)
            last_step(STEPS - 1)

        @block.scalar
        def _(act):
            def copy_out(step, entry, last=False):
                act.wait_ge(s_fill, filled(step, entry, last))
                bank = ring[bank_of(entry)]
                if entry[0] == "A":
                    out, src = embT[:, :, :, N_ROWS + entry[1]], bank[:, 0:PAIR, :]
                elif entry[0] == "T":
                    n = len(group_features(entry[2]))
                    at = entry[2] * GROUP
                    out, src = embT[:, entry[1], :, at:at + n], bank[:, 0:n, :].rearrange("p f b -> p b f")
                else:
                    out, src = pairsT[:, :, entry[1], :], bank[0:KP, 0:KT, :]
                nc.scalar.copy(out, src).then_inc(s_free, 1)

            def pack_pairs(step, slot):
                t = step * PAIR + slot
                act.wait_ge(s_gT, t + 1)
                nc.scalar.copy(gramT[:, slot, HALF + 1:N_FEAT, N_FEAT:TROW],
                               gramT[:, slot, HALF + 1:N_FEAT, 0:HALF]).then_inc(s_wrap, 1)
                act.wait_ge(s_wrap, t + 1)
                skew = gramT[:, slot, :, :].rearrange("p g f -> p (g f)")[:, 1:1 + N_FEAT * (TROW + 1)]
                nc.scalar.copy(pairs[:, slot, :].rearrange("p (g c) -> p g c", c=HALF),
                               skew.rearrange("p (g c) -> p g c", c=TROW + 1)[:, :, 0:HALF]).then_inc(s_pack, 1)

            def h1_relu(p, n, tiles):
                act.wait_ge(s_m1, p * NT1 + n + 1)
                nc.scalar.activation(h1_sb[:, n, 0:P * len(tiles)], mlp_ps[n % 2][:, 0:P * len(tiles)], ACT.Relu,
                                     bias=b1_sb[:, n:n + 1]).then_inc(s_h1, 1)

            def h2_relu(p, n, tiles):
                act.wait_ge(s_m2, p * NT2 + n + 1)
                nc.scalar.activation(h2_sb[:, n, 0:P * len(tiles)], mlp_ps[n][:, 0:P * len(tiles)], ACT.Relu,
                                     bias=b2_sb[:, n:n + 1]).then_inc(s_h2, 1)

            def y_out(p, out):
                act.wait_ge(s_m3, p + 1)
                nc.scalar.copy(out, mlp_ps[0][0:1, 0:out.shape[1]]).then_inc(s_y, 1)

            both = [0, 1]

            def y_out_step(step):
                y_out(step, y_sb[:, bass.ds(step, 1), :].rearrange("o s m -> o (s m)"))

            def first_tile(step, first):
                for entry in RING_T0:
                    copy_out(step, entry)
                if not first:
                    h2_relu(step - 1, 0, both)
                for j in range(EARLY_T1):
                    copy_out(step, ("T", 1, j))
                    if j == 1:
                        pack_pairs(step, 0)

            def step_of(step, first):
                first_tile(step, first)
                if not first:
                    h2_relu(step - 1, 1, both)
                copy_out(step, ("P", 0))
                for j in range(EARLY_T1, GROUPS):
                    copy_out(step, ("T", 1, j))
                pack_pairs(step, 1)
                copy_out(step + 1, ("A", 0))
                copy_out(step, ("P", 1))
                if not first:
                    y_out_step(step - 1)
                copy_out(step + 1, ("A", 1))
                h1_relu(step, 0, both)
                h1_relu(step, 1, both)
                copy_out(step + 1, ("A", 2))
                h1_relu(step, 2, both)
                h1_relu(step, 3, both)
                copy_out(step + 1, ("A", 3))

            def y_out_tile(p, step, tile):
                y_out(p, y_sb[:, step, tile * P:(tile + 1) * P])

            def last_step(step):
                first_tile(step, False)
                h2_relu(step - 1, 1, both)
                copy_out(step, ("P", 0))
                y_out_step(step - 1)
                for n in range(NT1):
                    h1_relu(step, n, [0])
                for j in range(EARLY_T1, GROUPS):
                    copy_out(step, ("T", 1, j))
                h2_relu(step, 0, [0])
                h2_relu(step, 1, [0])
                pack_pairs(step, 1)
                y_out_tile(step, step, 0)
                copy_out(step, ("P", 1), True)
                for n in range(NT1):
                    h1_relu(step + 1, n, [1])
                for n in range(NT2):
                    h2_relu(step + 1, n, [1])
                y_out_tile(step + 1, step, 1)

            for m, n in enumerate(OH_BLOCKS):
                act.wait_ge(s_tab[m % STAGES], 16 * (m // STAGES + 1))
                nc.scalar.copy(table_hi[:, OH_AT[m]:OH_AT[m] + n, :], staged[m % STAGES][:, 0:n, :]).then_inc(s_hi, 1)
                if 1 <= m <= len(AHEAD):
                    copy_out(0, ("A", m - 1))
            act.wait_ge(s_w, 16 * 6)
            step_of(0, True)
            with act.Fori(1, STEPS - 1) as step:
                step_of(step, False)
            last_step(STEPS - 1)

        @block.vector
        def _(dve):
            def make_onehot(step, m, first=False):
                n = OH_BLOCKS[m]
                dve.wait_ge(s_bc, nth(step, m))
                if not (first and m < 2):
                    before = (step, m - 2) if m >= 2 else (step - 1, max(k for k in range(len(OH)) if k % 2 == m % 2))
                    dve.wait_ge(s_fill, filled(before[0], ("A", before[1])))
                rows = row_ids_sb[:, BLOCK_KINDS.index(n), 0:n]
                nc.vector.tensor_tensor(
                    out=onehot[m % 2][:, 0:n, :],
                    in0=id_ps[0:ROWS_PER_BLOCK, 0:MB].unsqueeze(1).to_broadcast([ROWS_PER_BLOCK, n, MB]),
                    in1=rows.unsqueeze(2).to_broadcast([ROWS_PER_BLOCK, n, MB]),
                    op=ALU.is_equal).then_inc(s_oh, 1)

            def transpose_gram(step, slot):
                t = step * PAIR + slot
                dve.wait_ge(s_gram, t + 1)
                nc.vector.transpose(gramT[:, slot, 0:N_FEAT, 0:QUAD],
                                    gram_ps[:, :, 0:N_FEAT].rearrange("p q g -> p g q")).then_inc(s_gT, 1)

            def step_of(step, first):
                if not first:
                    for m in range(len(AHEAD) + 1, len(OH)):
                        make_onehot(step, m)
                make_onehot(step + 1, 0)
                transpose_gram(step, 0)
                transpose_gram(step, 1)
                for m in range(1, len(AHEAD) + 1):
                    make_onehot(step + 1, m)

            def last_step(step):
                for m in range(len(AHEAD) + 1, len(OH)):
                    make_onehot(step, m)
                transpose_gram(step, 0)
                transpose_gram(step, 1)

            def split_lo(m):
                n = OH_BLOCKS[m]
                dve.wait_ge(s_tab[m % STAGES], 16 * (m // STAGES + 1))
                dve.wait_ge(s_hi, m + 1)
                nc.vector.tensor_tensor(out=table_lo[:, OH_AT[m]:OH_AT[m] + n, :], in0=staged[m % STAGES][:, 0:n, :],
                                        in1=table_hi[:, OH_AT[m]:OH_AT[m] + n, :].bitcast(fp32), op=ALU.subtract).then_inc(s_lo, 1)

            nc.vector.memset(gram_ps[:, :, :], 0.0).then_inc(s_gz, 1)
            dve.wait_ge(s_ident, 1)
            nc.vector.tensor_copy(pick[:, :, :], ident[0:len(OH), 0:len(OH)].unsqueeze(2).to_broadcast(
                [len(OH), len(OH), ROWS_PER_BLOCK])).then_inc(s_pick, 1)
            dve.wait_ge(s_const, 32)
            nc.vector.tensor_copy(oh_ids_f[:, :, :].rearrange("f s m -> f (s m)"), oh_ids_sb).then_inc(s_pick, 1)
            for m in range(len(OH)):
                make_onehot(0, m, True)
                split_lo(m)
            step_of(0, True)
            with dve.Fori(1, STEPS - 1) as step:
                step_of(step, False)
            last_step(STEPS - 1)


def kernel(**inputs):
    import numpy as np
    import concourse.bacc as bacc
    from concourse import mybir as mb
    from concourse.bass_utils import run_bass_kernel_spmd as run

    nc = bacc.Bacc("TRN2", target_bir_lowering=False, num_devices=1)
    arrays = {}

    def dram_in(name, a):
        a = np.ascontiguousarray(a)
        arrays[name] = a
        return nc.dram_tensor(name, a.shape, mb.dt.from_np(a.dtype), kind="ExternalInput").ap()

    n_pairs = N_FEAT * HALF
    pair_row = {pair: i for i, pair in enumerate(zip(*(v.tolist() for v in np.triu_indices(N_FEAT, k=1))))}
    feature = [f + 1 for f in SLOTS]
    order = np.array([pair_row[tuple(sorted((feature[g], feature[(g + 1 + c) % N_FEAT])))]
                      for g in range(N_FEAT) for c in range(HALF)])
    row_ids = np.zeros((ROWS_PER_BLOCK, len(BLOCK_KINDS), MAX_BLOCKS), np.float32)
    for i, n in enumerate(BLOCK_KINDS):
        row_ids[:, i, :n] = np.arange(ROWS_PER_BLOCK * n).reshape(ROWS_PER_BLOCK, n)
    w1 = np.asarray(inputs["W_top1"])
    ids = np.asarray(inputs["ids"])
    args = [
        dram_in("bottom", inputs["r_bottom_output"]),
        dram_in("ids", ids[:, GATHERED].view(np.uint32).reshape(TILES, P, len(GATHERED)).transpose(1, 0, 2)),
        dram_in("oh_ids", ids[:, OH].T),
        [dram_in(f"tbl_{f}", inputs[f"tbl_{f}"]) for f in GATHERED],
        [dram_in(f"tbl_{f}", inputs[f"tbl_{f}"]) for f in OH],
        dram_in("row_ids", row_ids),
        dram_in("w1_pairs", w1[order]),
        dram_in("w1_bottom", w1[n_pairs:]),
        dram_in("b1", np.asarray(inputs["b_top1"]).reshape(NT1, P).T),
        dram_in("w2", inputs["W_top2"]),
        dram_in("b2", np.asarray(inputs["b_top2"]).reshape(NT2, P).T),
        dram_in("w3", np.asarray(inputs["W_top3"]).reshape(NT2, P).T),
    ]
    y = nc.dram_tensor("y", (BATCH, 1), mb.dt.float32, kind="ExternalOutput").ap()
    dlrm_tower(nc, *args, y)
    r = run(nc, [arrays], core_ids=[0])
    return r.results[0]["y"]
```

```python
import concourse.bass as bass
from concourse import mybir
from contextlib import ExitStack

BATCH = 2048
D = 128
N_TABLES = 26
N_FEAT = N_TABLES + 1
P = 128
TILES = BATCH // P
PAIR = 2
STEPS = TILES // PAIR
MB = PAIR * P
ROWS_PER_BLOCK = 125
ONE_HOT = {1: 1250, 2: 1250, 3: 1250, 4: 1250, 0: 1000, 20: 1000, 21: 1000, 25: 1000}
OH = list(ONE_HOT)
OH_BLOCKS = [ONE_HOT[f] // ROWS_PER_BLOCK for f in OH]
MAX_BLOCKS = max(OH_BLOCKS)
OH_AT = [sum(OH_BLOCKS[:m]) for m in range(len(OH))]
STAGES = 4
BLOCK_KINDS = sorted(set(OH_BLOCKS))
GATHERED = [f for f in range(N_TABLES) if f not in ONE_HOT]
SLOTS = [-1] + GATHERED + OH
N_ROWS = 1 + len(GATHERED)
GROUP = 4
GROUPS = -(-len(GATHERED) // GROUP)
LAST_GATHERED = 2
FPAD = 28
QUAD = 32
HALF = N_FEAT // 2
ROWS_PER_K = 9
KT = N_FEAT // ROWS_PER_K
KP = ROWS_PER_K * HALF
TROW = N_FEAT + HALF
H1, H2 = 512, 256
NT1 = H1 // P

AHEAD = [("A", m) for m in range(4)]
READ_AFTER = {1: [4], 2: [5], 3: [6], 4: [7]}
RING_T0 = [e for j in range(GROUPS) for e in [("T", 0, j)] + [("A", m) for m in READ_AFTER.get(j, [])]]
BEFORE_GRAM, BEFORE_MLP_END = 2, GROUPS - 1
RING = RING_T0 + [("T", 1, j) for j in range(GROUPS)] + AHEAD[:1] + [("P", 0)] + AHEAD[1:2] + [("P", 1)] + AHEAD[2:]
ENTRIES = len(RING)
NOT_IN_LAST = AHEAD + [("A", m) for m in range(len(OH) - LAST_GATHERED, len(OH))]
LAST_RING = [e for e in RING if e not in NOT_IN_LAST]
LAST_RING[-3:] = [("P", 0), ("T", 1, GROUPS - 1), ("P", 1)]
BANKS = 4
BANK = [i % BANKS for i in range(ENTRIES)]
if ENTRIES % BANKS == 1:
    BANK[-1] = 1


def group_features(j, last=False):
    assert len(GATHERED) + LAST_GATHERED <= GROUPS * GROUP
    rows = [(f - 1, f) for f in range(1 + j * GROUP, min(1 + (j + 1) * GROUP, N_ROWS))]
    if last and j == GROUPS - 1:
        rows += [(len(GATHERED) + i, N_FEAT - LAST_GATHERED + i) for i in range(LAST_GATHERED)]
    return rows


def is_last(step):
    return isinstance(step, int) and step == STEPS - 1


def bank_of(entry):
    return BANK[RING.index(entry)]


def filled(step, entry):
    if isinstance(step, int) and step == 0 and entry in AHEAD:
        return AHEAD.index(entry) + 1
    body = step - 1 if entry in AHEAD else step
    ring = LAST_RING if is_last(body) else RING
    return len(AHEAD) + ENTRIES * body + ring.index(entry) + 1


def freed(body, entry):
    ring = LAST_RING if is_last(body) else RING
    i = ring.index(entry)
    ahead_of_it = [k for k in range(i) if bank_of(ring[k]) == bank_of(entry)]
    if ahead_of_it:
        before = ahead_of_it[-1]
    elif isinstance(body, int) and body == 0:
        return max([n + 1 for n, e in enumerate(AHEAD) if bank_of(e) == bank_of(entry)], default=0)
    else:
        before = max(k for k in range(ENTRIES) if BANK[k] == bank_of(entry)) - ENTRIES
    return len(AHEAD) + ENTRIES * body + before + 1


def dlrm_tower(nc, bottom, ids, oh_ids, tables, oh_tables, row_ids, w1_pairs, w1_bottom, b1, w2, b2, w3, y):
    fp32, fp32r = mybir.dt.float32, mybir.dt.float32r
    ACT = mybir.ActivationFunctionType
    ALU = mybir.AluOpType
    ctx = ExitStack()
    with ctx:
        def sb(name, shape, dt=fp32):
            return ctx.enter_context(nc.sbuf_tensor(name, shape, dt))

        def ps(name, shape):
            return ctx.enter_context(nc.psum_tensor(name, shape, fp32))

        def sem(name):
            return ctx.enter_context(nc.semaphore(name))

        NG = len(GATHERED)
        ids_sb = sb("ids_sb", [P, PAIR, NG + LAST_GATHERED], mybir.dt.uint32)
        botT = sb("botT", [D, PAIR, P])
        emb = sb("emb", [P, PAIR, NG + LAST_GATHERED, D])
        embT = sb("embT", [D, PAIR, P, FPAD])
        gramT = sb("gramT", [P, PAIR, N_FEAT + 1, TROW])
        pairs = sb("pairs", [P, PAIR, KT * KP])
        pairsT = sb("pairsT", [KP, KT, PAIR, P])
        w1z_sb = sb("w1z_sb", [KP, KT, H1])
        w1b_sb = sb("w1b_sb", [D, H1])
        w2_sb = sb("w2_sb", [P, NT1, H2])
        w3_sb = sb("w3_sb", [P, H2])
        b1_sb = sb("b1_sb", [P, NT1])
        b2_sb = sb("b2_sb", [P, H2])
        h1_sb = sb("h1_sb", [P, NT1, MB])
        h2_sb = sb("h2_sb", [P, PAIR, H2])
        y_cols = sb("y_cols", [P, TILES])
        y_rows = sb("y_rows", [TILES, P])
        ident = sb("ident", [P, P])
        oh_ids_sb = sb("oh_ids_sb", [ROWS_PER_BLOCK, len(OH), MB], mybir.dt.int32)
        row_ids_sb = sb("row_ids_sb", [ROWS_PER_BLOCK, len(BLOCK_KINDS), MAX_BLOCKS])
        staged = [sb(f"staged{i}", [ROWS_PER_BLOCK, MAX_BLOCKS, D]) for i in range(STAGES)]
        table_hi = sb("table_hi", [ROWS_PER_BLOCK, sum(OH_BLOCKS), D], fp32r)
        table_lo = sb("table_lo", [ROWS_PER_BLOCK, sum(OH_BLOCKS), D], fp32r)
        onehot = [sb(f"onehot{i}", [ROWS_PER_BLOCK, MAX_BLOCKS, MB], fp32r) for i in range(2)]

        ring = [ps(f"ring{i}", [P, GROUP, P]) for i in range(BANKS)]
        gram_ps = ps("gram_ps", [P, QUAD, QUAD])
        mlp_ps = [ps(f"mlp_ps{i}", [P, 512]) for i in range(2)]

        s_ids = [sem(f"ids_loaded_{s}") for s in range(PAIR)]
        s_bot = sem("bottom_loaded")
        s_bot_in = sem("bottom_in_embT")
        s_const = sem("row_ids_loaded")
        s_oh_ids = [sem(f"one_hot_ids_loaded_{m}") for m in range(len(OH))]
        s_tab = [sem(f"table_staged_{i}") for i in range(STAGES)]
        s_w = sem("weights_loaded")
        s_id0 = sem("ident_zeroed")
        s_ident = sem("ident_ready")
        s_gz = sem("gram_psum_zeroed")
        s_emb = [[sem(f"gathered_{s}_{j}") for j in range(GROUPS)] for s in range(PAIR)]
        s_hi = sem("table_hi_ready")
        s_lo = sem("table_lo_ready")
        s_oh = sem("onehot_ready")
        s_fill = sem("ring_filled")
        s_free = sem("ring_copied_out")
        s_gram = sem("gram_done")
        s_gT = sem("gram_transposed")
        s_wrap = sem("gram_wrapped")
        s_pack = sem("pairs_packed")
        s_m1 = sem("h1_products")
        s_h1 = sem("h1_ready")
        s_m2 = sem("h2_products")
        s_h2 = sem("h2_biased")
        s_y = sem("y_ready")
        s_yT = sem("y_transposed")
        s_rows = sem("y_rows_ready")
        s_out = sem("y_stored")

        def mlp_bank(n, tiles):
            if tiles == [1]:
                return gram_ps[:, n * QUAD // 2:(n + 1) * QUAD // 2, :].rearrange("p q g -> p (q g)")
            return mlp_ps[n][:, :]

        def columns(tiles):
            return slice(tiles[0] * P, (tiles[-1] + 1) * P)

        def of_tile_0(step):
            return [e for e in RING_T0 if not (is_last(step) and e in NOT_IN_LAST)]

        def nth(step, m):
            return len(OH) * step + m + 1

        block = ctx.enter_context(nc.Block())

        @block.sync
        def _(sp):
            def load_tile(step, slot):
                t = step * PAIR + slot
                sp.dma_start(ids_sb[:, slot, :], ids[:, bass.ds(t, 1), :].rearrange("p t f -> p (t f)")).then_inc(s_ids[slot], 16)

            def load_bottom(step):
                sp.dma_start(botT[:, :, :].rearrange("d s b -> d (s b)"), bottom[:, bass.ds(step * MB, MB)]).then_inc(s_bot, 16)

            def load_oh_ids(step, m):
                sp.dma_start(oh_ids_sb[:, m, :], oh_ids[bass.ds(step, 1), m, :].to_broadcast([ROWS_PER_BLOCK, MB])).then_inc(s_oh_ids[m], 16)

            def reload_oh_ids(step, m):
                sp.wait_ge(s_oh, nth(step - 1, m))
                load_oh_ids(step, m)

            load_tile(0, 0)
            sp.dma_start(row_ids_sb[:, :, :], row_ids).then_inc(s_const, 16)
            for m, n in enumerate(OH_BLOCKS):
                load_oh_ids(0, m)
                if m >= STAGES:
                    sp.wait_ge(s_hi, m - STAGES + 1)
                    sp.wait_ge(s_lo, m - STAGES + 1)
                sp.dma_start(staged[m % STAGES][:, 0:n, :], oh_tables[m].rearrange("(p n) d -> p n d", n=n)).then_inc(s_tab[m % STAGES], 16)
                if m == 0:
                    load_tile(0, 1)
                    load_bottom(0)
            sp.dma_start(w1z_sb[:, :, :], w1_pairs.rearrange("(k p) n -> p k n", p=KP)).then_inc(s_w, 16)
            sp.dma_start(w1b_sb[:, :], w1_bottom).then_inc(s_w, 16)
            sp.dma_start(w2_sb[:, :, :], w2.rearrange("(k p) n -> p k n", p=P)).then_inc(s_w, 16)
            sp.dma_start(w3_sb[:, :], w3.to_broadcast([P, H2])).then_inc(s_w, 16)
            sp.dma_start(b1_sb[:, :], b1).then_inc(s_w, 16)
            sp.dma_start(b2_sb[:, :], b2.to_broadcast([P, H2])).then_inc(s_w, 16)

            def loads_of(step):
                for m in range(len(AHEAD) + 1, len(OH) - LAST_GATHERED if is_last(step) else len(OH)):
                    reload_oh_ids(step, m)
                for slot in range(PAIR):
                    sp.wait_ge(s_fill, filled(step - 1, ("T", slot, GROUPS - 1)))
                    load_tile(step, slot)

            def reload_bottom(step):
                sp.wait_ge(s_m1, step * NT1)
                load_bottom(step)

            for m in range(len(AHEAD) + 1):
                reload_oh_ids(1, m)
            with sp.Fori(1, STEPS - 1) as step:
                loads_of(step)
                reload_bottom(step)
                for m in range(len(AHEAD) + 1):
                    reload_oh_ids(step + 1, m)
            loads_of(STEPS - 1)
            reload_bottom(STEPS - 1)
            sp.wait_ge(s_rows, 1)
            sp.dma_start(y.rearrange("(t p) o -> t (p o)", p=P), y_rows[:, :]).then_inc(s_out, 16)
            sp.wait_ge(s_out, 16)

        @block.gpsimd
        def _(pool):
            pool.memset(ident[:, :], 0.0).then_inc(s_id0, 1)
            pool.wait_ge(s_id0, 1)
            pool.affine_select(out=ident[:, :], in_=ident[:, :], compare_op=ALU.not_equal, fill=1.0,
                               base=0, pattern=[[-1, P]], channel_multiplier=1).then_inc(s_ident, 1)

            def gather(step, slot, wait):
                pool.wait_ge(s_ids[slot], 16 * (step + 1))
                for j in range(GROUPS):
                    if wait:
                        pool.wait_ge(s_fill, filled(step - 1, ("T", slot, j)))
                        pool.nop(nofuse=True)
                    for row, _ in group_features(j, is_last(step)):
                        pool.indirect_dma_start(
                            out=emb[:, slot, row, :], out_offset=None, in_=tables[row],
                            in_offset=bass.IndirectOffsetOnAxis(ap=ids_sb[:, slot, row:row + 1], axis=0),
                        ).then_inc(s_emb[slot][j], 16)

            for slot in range(PAIR):
                gather(0, slot, False)
            with pool.Fori(1, STEPS - 1) as step:
                for slot in range(PAIR):
                    gather(step, slot, True)
            for slot in range(PAIR):
                gather(STEPS - 1, slot, True)

        @block.tensor
        def _(pe):
            def wait_bank(body, entry):
                n = freed(body, entry)
                if not (isinstance(n, int) and n == 0):
                    pe.wait_ge(s_free, n)

            def read_table(step, body, m, first=False):
                entry = ("A", m)
                pe.wait_ge(s_oh, nth(step, m))
                if first:
                    pe.wait_ge(s_lo, m + 1)
                    pe.wait_ge(s_hi, m + 1)
                if body is not None:
                    wait_bank(body, entry)
                else:
                    before = [k for k in range(m) if bank_of(("A", k)) == bank_of(entry)]
                    if before:
                        pe.wait_ge(s_free, before[-1] + 1)
                out = ring[bank_of(entry)][:, 0:PAIR, :].rearrange("p s b -> p (s b)")
                n = OH_BLOCKS[m]
                for b in range(n):
                    for part in (table_hi, table_lo):
                        last = pe.matmul(out, part[:, OH_AT[m] + b, :], onehot[m % 2][:, b, :],
                                         start=(b == 0 and part is table_hi), stop=(b == n - 1 and part is table_lo))
                last.then_inc(s_fill, 1)

            def transpose_group(step, slot, j):
                entry = ("T", slot, j)
                rows = group_features(j, is_last(step))
                pe.wait_ge(s_emb[slot][j], 16 * (len(group_features(j)) * step + len(rows)))
                wait_bank(step, entry)
                for i, (row, _) in enumerate(rows):
                    last = pe.transpose(ring[bank_of(entry)][:, i, :], emb[:, slot, row, :], ident[:, :])
                last.then_inc(s_fill, 1)

            def gram(step, slot, first):
                pe.wait_ge(s_free, filled(step, of_tile_0(step)[-1] if slot == 0 else ("T", 1, GROUPS - 1)))
                if slot == 0:
                    pe.wait_ge(s_bot_in, step + 1)
                if first and slot == 0:
                    pe.wait_ge(s_gz, 1)
                else:
                    pe.wait_ge(s_gT, step * PAIR + slot)
                for q in range(QUAD):
                    for s in range(P // QUAD):
                        e = embT[:, slot, s * QUAD + q, 0:N_FEAT]
                        last = pe.matmul(gram_ps[s * QUAD:s * QUAD + N_FEAT, q, 0:N_FEAT], e, e,
                                         start=True, stop=True)
                last.then_inc(s_gram, 1)

            def transpose_pairs(step, slot):
                entry = ("P", slot)
                pe.wait_ge(s_pack, step * PAIR + slot + 1)
                wait_bank(step, entry)
                for k in range(KT):
                    last = pe.transpose(ring[bank_of(entry)][0:KP, k, :], pairs[:, slot, k * KP:(k + 1) * KP], ident[:, :])
                last.then_inc(s_fill, 1)

            def h1_products(p, n, tiles, pairs_in=None, h2_before=None):
                at = slice(tiles[0], tiles[-1] + 1)
                for m in [0, 1] if n == 0 else [n] if n > 1 else []:
                    if m >= 2:
                        pe.wait_ge(s_h1, p * NT1 + m - 1)
                    elif h2_before is not None:
                        pe.wait_ge(s_h2, h2_before - 1 + m)
                    pe.matmul(mlp_bank(m % 2, tiles)[:, 0:P * len(tiles)], w1b_sb[:, m * P:(m + 1) * P],
                              botT[:, at, :].rearrange("d s b -> d (s b)"), start=True, stop=False)
                if n == 0:
                    pe.wait_ge(s_free, pairs_in)
                for k in range(KT):
                    last = pe.matmul(mlp_bank(n % 2, tiles)[:, 0:P * len(tiles)], w1z_sb[:, k, n * P:(n + 1) * P],
                                     pairsT[:, k, at, :].rearrange("p s b -> p (s b)"), start=False, stop=(k == KT - 1))
                last.then_inc(s_m1, 1)

            def h2_products(p, tile, tiles):
                bank = mlp_bank(tile - tiles[0], tiles)
                for k in range(NT1):
                    if tile == tiles[0] and k == 0:
                        pe.wait_ge(s_h1, (p + 1) * NT1 - 1)
                    if tile == tiles[0] and k == NT1 - 1:
                        pe.wait_ge(s_h1, (p + 1) * NT1)
                    last = pe.matmul(bank[:, 0:H2], h1_sb[:, k, columns([tile])], w2_sb[:, k, :],
                                     start=(k == 0), stop=(k == NT1 - 1))
                last.then_inc(s_m2, 1)

            both = [0, 1]

            def first_tile(step, first):
                entries = of_tile_0(step)
                for entry in entries:
                    if entry == entries[-1] and not first:
                        h2_products(step - 1, 0, both)
                    if entry[0] == "T":
                        transpose_group(step, 0, entry[2])
                    else:
                        read_table(step, step, entry[1], first)
                for j in range(BEFORE_GRAM):
                    transpose_group(step, 1, j)
                gram(step, 0, first)
                for j in range(BEFORE_GRAM, BEFORE_MLP_END):
                    transpose_group(step, 1, j)

            def step_of(step, first):
                first_tile(step, first)
                if not first:
                    h2_products(step - 1, 1, both)
                for j in range(BEFORE_MLP_END, GROUPS):
                    transpose_group(step, 1, j)
                read_table(step + 1, step, 0)
                gram(step, 1, first)
                transpose_pairs(step, 0)
                read_table(step + 1, step, 1)
                transpose_pairs(step, 1)
                if first:
                    pe.wait_ge(s_w, 16 * 6)
                h1_products(step, 0, both, filled(step, ("P", 1)), None if first else step * PAIR)
                h1_products(step, 1, both)
                read_table(step + 1, step, 2)
                h1_products(step, 2, both)
                h1_products(step, 3, both)
                read_table(step + 1, step, 3)

            def last_step(step):
                first_tile(step, False)
                h2_products(step - 1, 1, both)
                transpose_pairs(step, 0)
                h1_products(step, 0, [0], filled(step, ("P", 0)), step * PAIR)
                h1_products(step, 1, [0])
                for j in range(BEFORE_MLP_END, GROUPS):
                    transpose_group(step, 1, j)
                h1_products(step, 2, [0])
                gram(step, 1, False)
                h1_products(step, 3, [0])
                h2_products(step, 0, [0])
                transpose_pairs(step, 1)
                for n in range(NT1):
                    h1_products(step + 1, n, [1], filled(step, ("P", 1)))
                h2_products(step + 1, 1, [1])

            pe.wait_ge(s_ident, 1)
            for m in range(len(AHEAD)):
                read_table(0, None, m, True)
            step_of(0, True)
            with pe.Fori(1, STEPS - 1) as step:
                step_of(step, False)
            last_step(STEPS - 1)
            pe.wait_ge(s_y, TILES)
            pe.transpose(mlp_ps[1][0:TILES, 0:P], y_cols[:, :], ident[:, :]).then_inc(s_yT, 1)

        @block.scalar
        def _(act):
            def copy_out(step, entry):
                act.wait_ge(s_fill, filled(step, entry))
                bank = ring[bank_of(entry)]
                if entry[0] == "A":
                    out, src = embT[:, :, :, N_ROWS + entry[1]], bank[:, 0:PAIR, :]
                elif entry[0] == "T":
                    rows = group_features(entry[2], is_last(step))
                    n = len(group_features(entry[2]))
                    if len(rows) > n:
                        at = rows[n][1]
                        nc.scalar.copy(embT[:, entry[1], :, at:at + len(rows) - n],
                                       bank[:, n:len(rows), :].rearrange("p f b -> p b f"))
                    at = rows[0][1]
                    out, src = embT[:, entry[1], :, at:at + n], bank[:, 0:n, :].rearrange("p f b -> p b f")
                else:
                    out, src = pairsT[:, :, entry[1], :], bank[0:KP, 0:KT, :]
                nc.scalar.copy(out, src).then_inc(s_free, 1)

            def pack_pairs(step, slot):
                t = step * PAIR + slot
                act.wait_ge(s_gT, t + 1)
                nc.scalar.copy(gramT[:, slot, HALF + 1:N_FEAT, N_FEAT:TROW],
                               gramT[:, slot, HALF + 1:N_FEAT, 0:HALF]).then_inc(s_wrap, 1)
                act.wait_ge(s_wrap, t + 1)
                skew = gramT[:, slot, :, :].rearrange("p g f -> p (g f)")[:, 1:1 + N_FEAT * (TROW + 1)]
                nc.scalar.copy(pairs[:, slot, :].rearrange("p (g c) -> p g c", c=HALF),
                               skew.rearrange("p (g c) -> p g c", c=TROW + 1)[:, :, 0:HALF]).then_inc(s_pack, 1)

            def h1_relu(p, n, tiles):
                act.wait_ge(s_m1, p * NT1 + n + 1)
                nc.scalar.activation(h1_sb[:, n, columns(tiles)], mlp_bank(n % 2, tiles)[:, 0:P * len(tiles)], ACT.Relu,
                                     bias=b1_sb[:, n:n + 1]).then_inc(s_h1, 1)

            both = [0, 1]

            def bottom_in(step):
                act.wait_ge(s_bot, 16 * (step + 1))
                nc.scalar.copy(embT[:, :, :, 0], botT[:, :, :]).then_inc(s_bot_in, 1)

            def first_tile(step, first):
                bottom_in(step)
                for entry in of_tile_0(step):
                    copy_out(step, entry)
                for j in range(BEFORE_MLP_END):
                    copy_out(step, ("T", 1, j))

            def step_of(step, first):
                first_tile(step, first)
                for j in range(BEFORE_MLP_END, GROUPS):
                    copy_out(step, ("T", 1, j))
                pack_pairs(step, 0)
                pack_pairs(step, 1)
                copy_out(step + 1, ("A", 0))
                copy_out(step, ("P", 0))
                copy_out(step + 1, ("A", 1))
                copy_out(step, ("P", 1))
                if first:
                    act.wait_ge(s_w, 16 * 6)
                h1_relu(step, 0, both)
                h1_relu(step, 1, both)
                copy_out(step + 1, ("A", 2))
                h1_relu(step, 2, both)
                h1_relu(step, 3, both)
                copy_out(step + 1, ("A", 3))

            def last_step(step):
                first_tile(step, False)
                pack_pairs(step, 0)
                copy_out(step, ("P", 0))
                h1_relu(step, 0, [0])
                h1_relu(step, 1, [0])
                for j in range(BEFORE_MLP_END, GROUPS):
                    copy_out(step, ("T", 1, j))
                h1_relu(step, 2, [0])
                h1_relu(step, 3, [0])
                pack_pairs(step, 1)
                copy_out(step, ("P", 1))
                for n in range(NT1):
                    h1_relu(step + 1, n, [1])

            for m, n in enumerate(OH_BLOCKS):
                act.wait_ge(s_tab[m % STAGES], 16 * (m // STAGES + 1))
                nc.scalar.copy(table_hi[:, OH_AT[m]:OH_AT[m] + n, :], staged[m % STAGES][:, 0:n, :]).then_inc(s_hi, 1)
                if m + 1 >= STAGES and m + 1 - STAGES < len(AHEAD):
                    copy_out(0, ("A", m + 1 - STAGES))
            step_of(0, True)
            with act.Fori(1, STEPS - 1) as step:
                step_of(step, False)
            last_step(STEPS - 1)
            act.wait_ge(s_yT, 1)
            nc.scalar.copy(y_rows[:, :], mlp_ps[1][0:TILES, 0:P]).then_inc(s_rows, 1)

        @block.vector
        def _(dve):
            def make_onehot(step, m, first=False):
                n = OH_BLOCKS[m]
                dve.wait_ge(s_oh_ids[m], 16 * (step + 1))
                if not (first and m < 2):
                    before = (step, m - 2) if m >= 2 else (step - 1, max(k for k in range(len(OH)) if k % 2 == m % 2))
                    dve.wait_ge(s_fill, filled(before[0], ("A", before[1])))
                rows = row_ids_sb[:, BLOCK_KINDS.index(n), 0:n]
                nc.vector.tensor_tensor(
                    out=onehot[m % 2][:, 0:n, :],
                    in0=oh_ids_sb[:, m, :].unsqueeze(1).to_broadcast([ROWS_PER_BLOCK, n, MB]),
                    in1=rows.unsqueeze(2).to_broadcast([ROWS_PER_BLOCK, n, MB]),
                    op=ALU.is_equal).then_inc(s_oh, 1)

            def transpose_gram(step, slot):
                t = step * PAIR + slot
                dve.wait_ge(s_gram, t + 1)
                nc.vector.transpose(gramT[:, slot, 0:N_FEAT, 0:QUAD],
                                    gram_ps[:, :, 0:N_FEAT].rearrange("p q g -> p g q")).then_inc(s_gT, 1)

            def y_of(step, slot, tiles):
                t = step * PAIR + slot
                dve.wait_ge(s_m2, t + 1)
                nc.vector.tensor_tensor(out=h2_sb[:, slot, :], in0=mlp_bank(slot - tiles[0], tiles)[:, 0:H2],
                                        in1=b2_sb[:, :], op=ALU.add).then_inc(s_h2, 1)
                dve.wait_ge(s_h2, t + 1)
                nc.vector.scalar_tensor_tensor(out=h2_sb[:, slot, :], in0=h2_sb[:, slot, :], scalar=0.0, in1=w3_sb[:, :],
                                               op0=ALU.max, op1=ALU.mult, accum_out=y_cols[:, bass.ds(t, 1)]).then_inc(s_y, 1)

            both = [0, 1]

            def step_of(step, first):
                if not first:
                    for m in range(len(AHEAD) + 1, len(OH)):
                        make_onehot(step, m)
                    y_of(step - 1, 0, both)
                make_onehot(step + 1, 0)
                transpose_gram(step, 0)
                make_onehot(step + 1, 1)
                if not first:
                    y_of(step - 1, 1, both)
                transpose_gram(step, 1)
                for m in range(2, len(AHEAD) + 1):
                    make_onehot(step + 1, m)

            def last_step(step):
                for m in range(len(AHEAD) + 1, len(OH) - LAST_GATHERED):
                    make_onehot(step, m)
                y_of(step - 1, 0, both)
                transpose_gram(step, 0)
                y_of(step - 1, 1, both)
                transpose_gram(step, 1)
                y_of(step, 0, [0])
                y_of(step, 1, [1])

            def split_lo(m):
                n = OH_BLOCKS[m]
                dve.wait_ge(s_tab[m % STAGES], 16 * (m // STAGES + 1))
                dve.wait_ge(s_hi, m + 1)
                nc.vector.tensor_tensor(out=table_lo[:, OH_AT[m]:OH_AT[m] + n, :], in0=staged[m % STAGES][:, 0:n, :],
                                        in1=table_hi[:, OH_AT[m]:OH_AT[m] + n, :].bitcast(fp32), op=ALU.subtract).then_inc(s_lo, 1)

            nc.vector.memset(gram_ps[:, :, :], 0.0).then_inc(s_gz, 1)
            dve.wait_ge(s_const, 16)
            for m in range(len(OH)):
                make_onehot(0, m, True)
                split_lo(m)
            step_of(0, True)
            dve.wait_ge(s_w, 16 * 6)
            with dve.Fori(1, STEPS - 1) as step:
                step_of(step, False)
            last_step(STEPS - 1)


def kernel(**inputs):
    import numpy as np
    import concourse.bacc as bacc
    from concourse import mybir as mb
    from concourse.bass_utils import run_bass_kernel_spmd as run

    nc = bacc.Bacc("TRN2", target_bir_lowering=False, num_devices=1)
    arrays = {}

    def dram_in(name, a):
        a = np.ascontiguousarray(a)
        arrays[name] = a
        return nc.dram_tensor(name, a.shape, mb.dt.from_np(a.dtype), kind="ExternalInput").ap()

    n_pairs = N_FEAT * HALF
    pair_row = {pair: i for i, pair in enumerate(zip(*(v.tolist() for v in np.triu_indices(N_FEAT, k=1))))}
    feature = [f + 1 for f in SLOTS]
    order = np.array([pair_row[tuple(sorted((feature[g], feature[(g + 1 + c) % N_FEAT])))]
                      for g in range(N_FEAT) for c in range(HALF)])
    row_ids = np.zeros((ROWS_PER_BLOCK, len(BLOCK_KINDS), MAX_BLOCKS), np.float32)
    for i, n in enumerate(BLOCK_KINDS):
        row_ids[:, i, :n] = np.arange(ROWS_PER_BLOCK * n).reshape(ROWS_PER_BLOCK, n)
    w1 = np.asarray(inputs["W_top1"])
    ids = np.asarray(inputs["ids"])
    by_row = GATHERED + OH[len(OH) - LAST_GATHERED:]
    tables = {f: dram_in(f"tbl_{f}", inputs[f"tbl_{f}"]) for f in range(N_TABLES)}
    args = [
        dram_in("bottom", np.asarray(inputs["r_bottom_output"]).T),
        dram_in("ids", ids[:, by_row].view(np.uint32).reshape(TILES, P, len(by_row)).transpose(1, 0, 2)),
        dram_in("oh_ids", ids[:, OH].reshape(STEPS, MB, len(OH)).transpose(0, 2, 1)),
        [tables[f] for f in by_row],
        [tables[f] for f in OH],
        dram_in("row_ids", row_ids),
        dram_in("w1_pairs", w1[order]),
        dram_in("w1_bottom", w1[n_pairs:]),
        dram_in("b1", np.asarray(inputs["b_top1"]).reshape(NT1, P).T),
        dram_in("w2", inputs["W_top2"]),
        dram_in("b2", np.asarray(inputs["b_top2"]).reshape(1, H2)),
        dram_in("w3", np.asarray(inputs["W_top3"]).reshape(1, H2)),
    ]
    y = nc.dram_tensor("y", (BATCH, 1), mb.dt.float32, kind="ExternalOutput").ap()
    dlrm_tower(nc, *args, y)
    r = run(nc, [arrays], core_ids=[0])
    return r.results[0]["y"]
```
